# Optimizing a Trainium2 kernel written in Bass

```python
import numpy as np
import jax
import jax.numpy as jnp

def _softmax(x, axis=-1):
    return jax.nn.softmax(x, axis=axis)

def _gelu(x):
    return jax.nn.gelu(x, approximate=True)

def _silu(x):
    return jax.nn.silu(x)

def _sigmoid(x):
    return jax.nn.sigmoid(x)

def _layernorm(x, axis=-1, eps=1e-05):
    m = jnp.mean(x, axis=axis, keepdims=True)
    v = jnp.var(x, axis=axis, keepdims=True)
    return (x - m) / jnp.sqrt(v + eps)

def _scatter_add(tgt, idx, src, axis=0):
    return tgt.at[idx].add(src)

def _segment_sum(src, seg, n):
    return jax.ops.segment_sum(src, seg, n)
kernel_name = 'mk_flamingo_gated_d1_seqx_r4_511070'

def setup_inputs(seed: int=0):
    np.random.seed(seed)
    _w = jnp.asarray

    def _rec_inputs():
        import jax
        import jax.numpy as jnp
        _rk = jax.random.key(seed)
        x = 7.22e-05 + 1 * jax.random.normal(jax.random.fold_in(_rk, 1), (2, 1024, 256), jnp.float32)
        _lenS = 1024 - jax.random.randint(jax.random.fold_in(_rk, 7), (2,), 0, max(1, 1024 // 4) + 1, jnp.int32)
        _lenS2 = 154 - jax.random.randint(jax.random.fold_in(_rk, 8), (2,), 0, max(1, 154 // 4) + 1, jnp.int32)
        _ctx_1024P = jax.random.normal(jax.random.fold_in(_rk, 11), (2, 16, 256), jnp.float32)
        _ctx_1024c = jax.random.dirichlet(jax.random.fold_in(_rk, 511), 0.3 * jnp.ones((16,), jnp.float32), (2, 154))
        _ctx_1024t = jnp.einsum('bsk,bkd->bsd', _ctx_1024c, _ctx_1024P)
        _ctx_1024t = _ctx_1024t * jax.lax.rsqrt(jnp.mean(jnp.square(_ctx_1024t)) + 1e-12) * 0.953939
        ctx_1024 = 4.13588e-05 + 0.999923 * (_ctx_1024t + 0.3 * jax.random.normal(jax.random.fold_in(_rk, 611), (2, 154, 256), jnp.float32))
        _validS = jnp.arange(1024)[None, :] < _lenS[:, None]
        _validS2 = jnp.arange(154)[None, :] < _lenS2[:, None]
        _causal = jnp.tril(jnp.ones((1024, 1024), dtype=bool))
        mask_1x1xSxS2_ik1 = jnp.where(jnp.broadcast_to(_validS2[0:1, None, None, :], (1, 1, 1024, 154)), 1, 0).astype(jnp.int32)
        _g = jax.random.normal(jax.random.fold_in(_rk, 9001), (2, 1), jnp.float32)
        _g = jnp.sign(_g) * jnp.maximum(jnp.abs(_g), 1.0) + (_g == 0) * 1.0
        g_xattn = _g[0]
        g_ffn = _g[1]
        return (x, ctx_1024, mask_1x1xSxS2_ik1, g_xattn, g_ffn)
    x, ctx_1024, mask_1x1xSxS2_ik1, g_xattn, g_ffn = _rec_inputs()

    def _L0_xattn_setup():
        import jax, jax.numpy as jnp
        import numpy as np
        D_MODEL = 256
        NUM_HEADS = 16
        D_K = D_MODEL // NUM_HEADS
        B, S = (4, 512)
        key = jax.random.key(seed)
        ks = jax.random.split(key, 12)
        std = 1.0 / np.sqrt(D_MODEL)
        mk = lambda k: jax.random.normal(k, (D_MODEL, D_MODEL), jnp.float32) * std
        return {'q': jax.random.normal(ks[0], (B, S, D_MODEL), jnp.float32), 'k': jax.random.normal(ks[1], (B, S, D_MODEL), jnp.float32), 'v': jax.random.normal(ks[2], (B, S, D_MODEL), jnp.float32), 'mask': jax.random.randint(ks[3], (1, 1, S, S), 0, 2, jnp.int32), 'Wq': mk(ks[4]), 'bq': jnp.zeros((D_MODEL,), jnp.float32), 'Wk': mk(ks[5]), 'bk': jnp.zeros((D_MODEL,), jnp.float32), 'Wv': mk(ks[6]), 'bv': jnp.zeros((D_MODEL,), jnp.float32), 'Wo': mk(ks[7]), 'bo': jnp.zeros((D_MODEL,), jnp.float32)}
    _L0_xattn_all = _L0_xattn_setup()
    _L0_xattn_in = {k: v for k, v in _L0_xattn_all.items() if k in ('Wq', 'bq', 'Wk', 'bk', 'Wv', 'bv', 'Wo', 'bo')}
    del _L0_xattn_all

    def _L0_ffn_setup():
        import math
        import jax, jax.numpy as jnp
        import numpy as np
        B, S, D, H, E, K = (4, 512, 256, 1024, 8, 2)
        CAPACITY_RATIO = 1.05
        key = jax.random.key(seed)
        k0, k1, k2, k3 = jax.random.split(key, 4)
        x = jax.random.normal(k0, (B, S, D), jnp.float32)
        Wg = jax.random.normal(k1, (D, E), jnp.float32) * 0.02
        W1 = jax.random.normal(k2, (E, D, H), jnp.float32) * 0.02
        b1 = jnp.zeros((E, H), jnp.float32)
        W2 = jax.random.normal(k3, (E, H, D), jnp.float32) * 0.02
        b2 = jnp.zeros((E, D), jnp.float32)
        return {'x': x, 'Wg': Wg, 'W1': W1, 'b1': b1, 'W2': W2, 'b2': b2}
    _L0_ffn_all = _L0_ffn_setup()
    _L0_ffn_in = {k: v for k, v in _L0_ffn_all.items() if k in ('Wg', 'W1', 'b1', 'W2', 'b2')}
    del _L0_ffn_all
    return {'x': x, 'ctx_1024': ctx_1024, 'mask_1x1xSxS2_ik1': mask_1x1xSxS2_ik1, 'g_xattn': g_xattn, 'g_ffn': g_ffn, 'L0_xattn_Wq': _L0_xattn_in['Wq'], 'L0_xattn_bq': _L0_xattn_in['bq'], 'L0_xattn_Wk': _L0_xattn_in['Wk'], 'L0_xattn_bk': _L0_xattn_in['bk'], 'L0_xattn_Wv': _L0_xattn_in['Wv'], 'L0_xattn_bv': _L0_xattn_in['bv'], 'L0_xattn_Wo': _L0_xattn_in['Wo'], 'L0_xattn_bo': _L0_xattn_in['bo'], 'L0_ffn_Wg': _L0_ffn_in['Wg'], 'L0_ffn_W1': _L0_ffn_in['W1'], 'L0_ffn_b1': _L0_ffn_in['b1'], 'L0_ffn_W2': _L0_ffn_in['W2'], 'L0_ffn_b2': _L0_ffn_in['b2']}

def reference(x, ctx_1024, mask_1x1xSxS2_ik1, g_xattn, g_ffn, L0_xattn_Wq, L0_xattn_bq, L0_xattn_Wk, L0_xattn_bk, L0_xattn_Wv, L0_xattn_bv, L0_xattn_Wo, L0_xattn_bo, L0_ffn_Wg, L0_ffn_W1, L0_ffn_b1, L0_ffn_W2, L0_ffn_b2):
    import jax
    import jax.numpy as jnp

    def _L0_xattn_ref(q, k, v, mask, Wq, bq, Wk, bk, Wv, bv, Wo, bo):
        import jax, jax.numpy as jnp
        import numpy as np
        D_MODEL = 256
        NUM_HEADS = 16
        D_K = D_MODEL // NUM_HEADS
        B, S = (4, 512)
        N = q.shape[0]

        def proj(x, W, b):
            y = x @ W.T + b
            return y.reshape(N, -1, NUM_HEADS, D_K).transpose(0, 2, 1, 3)
        qh, kh, vh = (proj(q, Wq, bq), proj(k, Wk, bk), proj(v, Wv, bv))
        scores = jnp.einsum('bhqd,bhkd->bhqk', qh, kh) / jnp.sqrt(jnp.float32(D_K))
        scores = jnp.where(mask == 0, jnp.float32(-1000000000.0), scores)
        attn = jax.nn.softmax(scores, axis=-1)
        x = jnp.einsum('bhqk,bhkd->bhqd', attn, vh)
        x = x.transpose(0, 2, 1, 3).reshape(N, -1, NUM_HEADS * D_K)
        return x @ Wo.T + bo

    def _L0_ffn_ref(x, Wg, W1, b1, W2, b2):
        import math
        import jax, jax.numpy as jnp
        import numpy as np
        B, S, D, H, E, K = (4, 512, 256, 1024, 8, 2)
        CAPACITY_RATIO = 1.05
        b, s, d = x.shape
        e = Wg.shape[1]
        n = b * s
        cap = int(math.ceil(n * K / e * CAPACITY_RATIO))
        xf = x.reshape(n, d)
        probs = jax.nn.softmax(xf @ Wg, axis=-1)
        topv, topi = jax.lax.top_k(probs, K)
        gates = topv / jnp.sum(topv, axis=-1, keepdims=True)
        eidx = topi.reshape(-1)
        oh = jax.nn.one_hot(eidx, e, dtype=jnp.int32)
        pos = jnp.sum(jnp.cumsum(oh, axis=0) * oh, axis=-1) - 1
        keep = pos < cap
        dest = jnp.where(keep, eidx * cap + pos, e * cap)
        xr = jnp.repeat(xf, K, axis=0)
        buf = jnp.zeros((e * cap + 1, d), x.dtype).at[dest].set(xr)
        expert_in = buf[:e * cap].reshape(e, cap, d)
        h = jax.nn.gelu(jnp.einsum('ecd,edh->ech', expert_in, W1) + b1[:, None, :])
        y = jnp.einsum('ech,ehd->ecd', h, W2) + b2[:, None, :]
        yf = jnp.concatenate([y.reshape(e * cap, d), jnp.zeros((1, d), y.dtype)], axis=0)
        gathered = yf[dest]
        w = (gates.reshape(-1) * keep.astype(gates.dtype))[:, None]
        out = (gathered * w).reshape(n, K, d).sum(axis=1).reshape(b, s, d)
        return out
    x = x + jnp.tanh(g_xattn[0]) * _L0_xattn_ref(_layernorm(x, axis=-1), ctx_1024, ctx_1024, mask_1x1xSxS2_ik1, L0_xattn_Wq, L0_xattn_bq, L0_xattn_Wk, L0_xattn_bk, L0_xattn_Wv, L0_xattn_bv, L0_xattn_Wo, L0_xattn_bo)
    x = x + jnp.tanh(g_ffn[0]) * _L0_ffn_ref(_layernorm(x, axis=-1), L0_ffn_Wg, L0_ffn_W1, L0_ffn_b1, L0_ffn_W2, L0_ffn_b2)
    return x

_drawn_inputs = setup_inputs


def setup_inputs(seed=0):
    import zlib

    import numpy as np

    out = dict(_drawn_inputs(seed))
    spreads = {'L0_xattn_bq': (0.0, 0.388),
     'L0_xattn_bk': (0.0, 0.8),
     'L0_xattn_bv': (0.0, 0.1),
     'L0_xattn_bo': (0.0, 0.1),
     'L0_ffn_b1': (0.0, 0.384),
     'L0_ffn_b2': (0.0, 0.1)}
    factors = {}
    for name, (base, spread) in spreads.items():
        noise = np.random.default_rng([zlib.crc32(name.encode()), seed]).standard_normal(out[name].shape)
        drawn = base * np.exp(spread * noise) if base else spread * noise
        out[name] = jnp.asarray(drawn.astype(out[name].dtype))
    for name, factor in factors.items():
        out[name] = (out[name] * factor).astype(out[name].dtype)
    return out
```

```python
from contextlib import ExitStack

import numpy as np

import concourse.bass as bass
from concourse import mybir

F32 = mybir.dt.float32
BF16 = mybir.dt.bfloat16
I32 = mybir.dt.int32
U32 = mybir.dt.uint32
ALU = mybir.AluOpType
ACT = mybir.ActivationFunctionType
AX = mybir.AxisListType

B, S, D = 2, 1024, 256
KEYS = 154
HEADS, DK = 16, 16
E, HID = 8, 1024
TOK = B * S
CAP = -(-(TOK * 2 * 105) // (E * 100))
EPS = 1e-5
BIG = float(2.0 ** 100)

P = 128
KD = D // P
PAIRS = HEADS // 2
QC = 512
NCH = TOK // QC
QT = QC // P
ROWS = 103
PK = 3 * ROWS
VW = 66
NT = TOK // P
XW = 260
SLOT = 108
ST5 = 5
LAST = CAP - 4 * SLOT
NSLOT = E * CAP
HM = HID // P
CA = 270
CB = CAP - CA

MX, SC, PVB, MISC = (0, 1), (2, 3, 4), 5, (6, 7)
H_BANK, Y_BANK, T_BANK = (0, 1, 2, 3), (4, 5), (6, 7)


def misc_turns():
    order = [("k", 0), ("k", 1), ("xt", 0, 0), ("xt", 0, 1), ("q", 0, 0), ("q", 0, 1)]
    order += [("v", i) for i in range(3)] + [("m", 0)]
    for c in range(NCH):
        for j in range(PAIRS):
            order += [u for u in misc_uses(c, j)]
    order += post_uses(NCH - 1, None)
    return {name: (n % 2, n // 2) for n, name in enumerate(order)}, order


def post_uses(c, j):
    steps = {1: [("at", c, 0), ("at", c, 1)], 2: [("wo", c, 0), ("wo", c, 1)],
             4: [("x2t", c, 0), ("x2t", c, 1)], 5: [("lg", c)], 7: [("pos", c)]}
    if j is None:
        return [u for s in sorted(steps) for u in steps[s]]
    return steps.get(j, [])


def misc_uses(c, j):
    out = []
    if c + 1 < NCH:
        out += {0: [("xt", c + 1, 0), ("xt", c + 1, 1)], 1: [("q", c + 1, 0), ("q", c + 1, 1)],
                7: [("m", c + 1)]}.get(j, [])
    if c == 0 and j == 2:
        out += [("v", i) for i in range(3, 6)]
    if c >= 1:
        out += post_uses(c - 1, j)
    return out


def bcast(row, n):
    return row.rearrange("(o d) -> o d", o=1).to_broadcast([n, row.shape[0]])


def hi(ap):
    v = ap.bitcast(BF16)
    n = len(v.shape)
    if n == 2:
        return v[:, 1::2]
    if n == 3:
        return v[:, :, 1::2]
    return v[:, :, :, 1::2]


def build(nc, a):
    ctx = ExitStack()
    with ctx:
        def sb(name, shape, dt):
            return ctx.enter_context(nc.sbuf_tensor(name, shape, dt))

        def sem(name):
            return ctx.enter_context(nc.semaphore(name))

        def sems(name, n):
            return [sem(f"{name}{i}") for i in range(n)]

        ps = ctx.enter_context(nc.psum_tensor("ps", [P, 8, 512], F32))

        kq = [nc.dram_tensor(n, (D, 2 * KEYS), BF16, kind="Internal").ap() for n in ("k_high", "k_low")]
        qd = [nc.dram_tensor(n, (D, TOK), BF16, kind="Internal").ap() for n in ("q_high", "q_low")]
        rows = nc.dram_tensor("expert_rows", (NSLOT + 2 * TOK, XW), F32, kind="Internal").ap()

        idf = sb("idf", [P, P], F32)
        idb = sb("idb", [P, P], BF16)
        trif = sb("trif", [P, P], F32)
        trib = sb("trib", [P, P], BF16)
        onesb = sb("onesb", [P, P], BF16)
        small = sb("small", [P, 128], F32)
        tokid = sb("tokid", [P, NT], I32)
        dumpf = sb("dumpf", [P, 2, NT], F32)
        b1T = sb("b1T", [P, E * HM], F32)
        b1c = sb("b1c", [P, 2, HM], F32)
        b2B = sb("b2B", [P, E * D], F32)
        bvB = sb("bvB", [P, D], F32)
        boB = sb("boB", [P, D], F32)
        wgf = sb("wgf", [P, KD, E], F32)
        wg16 = sb("wg16", [P, KD, 2 * E], BF16)
        wq = sb("wq", [P, KD, D], F32)
        wk = sb("wk", [P, KD, D], F32)
        wv = sb("wv", [P, KD, D], F32)
        wo = sb("wo", [P, KD, D], F32)
        wql = sb("wql", [P, KD, D], BF16)
        wol = sb("wol", [P, KD, D], BF16)
        bq, bk = small[:, 0:2], small[:, 2:4]
        tgx, tgf = small[:, 6:7], small[:, 7:8]
        rank = small[:, 8:16]
        half = small[:, 24:28]

        ctxT = sb("ctxT", [P, KD, B, PK], F32)
        khl = sb("khl", [P, 2, 2, 2 * KEYS], BF16)
        ks = sb("ks", [P, B, PAIRS, PK + 1], BF16)
        vf = sb("vf", [ROWS, D], F32)
        vs = sb("vs", [ROWS, B, 3, PAIRS, VW], BF16)
        mqi = sb("mqi", [P, 8, KEYS], I32)
        mti = sb("mti", [P, 3, S], I32)
        mq = sb("mq", [P, 8, KEYS], BF16)
        mt = sb("mt", [ROWS, 3, S], BF16)
        x = sb("x", [P, NT, D], F32)
        st6 = sb("st6", [P, QT, 6], F32)
        mv = sb("mv", [P, QT, 2], F32)
        ve = sb("ve", [P, QT], F32)
        rstd = sb("rstd", [P, QT], F32)
        xn = sb("xn", [P, QT, D], F32)
        xt = sb("xt", [P, KD, QC], F32)
        xtl = sb("xtl", [P, KD, QC], BF16)
        qhl = sb("qhl", [P, 2, KD, QC], BF16)
        qs = sb("qs", [P, 2, PAIRS, QC], BF16)
        nm = sb("nm", [P, QT, HEADS], F32)
        mp = sb("mp", [P, QT, P], BF16)
        p32 = sb("p32", [P, 2, 3, QC], F32)
        pl = sb("pl", [ROWS, 2, 3, QC], BF16)
        ou = sb("ou", [P, QT * PAIRS, VW], F32)
        rd = sb("rd", [P, QT * PAIRS, 2], F32)
        at = sb("at", [P, QT * PAIRS, 2, DK], F32)
        att = sb("att", [P, KD, QC], F32)
        atl = sb("atl", [P, KD, QC], BF16)
        x2 = sb("x2", [P, QT, D], F32)
        mv2 = sb("mv2", [P, QT, 2], F32)
        ve2 = sb("ve2", [P, QT], F32)
        rstd2 = sb("rstd2", [P, QT], F32)
        st62 = sb("st62", [P, QT, 6], F32)
        xs = sb("xs", [P, 2, QT, XW], F32)
        x2t, x2l = att, atl
        lg16 = sb("lg16", [P, QT, 2 * E], F32)
        lg = sb("lg", [P, QT, E], F32)
        lgb = sb("lgb", [P, QT, E], F32)
        l12 = sb("l12", [P, 2, QT], F32)
        eqs = sb("eqs", [P, QT, E], F32)
        s12 = sb("s12", [P, 2, QT], F32)
        m12 = sb("m12", [P, 2, QT, E], F32)
        msum = sb("msum", [P, QT, E], BF16)
        mcum = sb("mcum", [P, QT, E], BF16)
        carry = sb("carry", [P, E], BF16)
        pmk = sb("pmk", [P, 2, QT, E], F32)
        posk = sb("posk", [P, 2, QT], F32)
        keep = sb("keep", [P, 2, QT], F32)
        dst = sb("dst", [P, 2, QT], F32)
        dsti = sb("dsti", [P, 2, NT], I32)
        gd = sb("gd", [P, QT], F32)
        gx = sb("gx", [P, QT], F32)
        gr = sb("gr", [P, QT], F32)
        w1 = sb("w1", [P, 2, KD, HID], F32)
        w2 = sb("w2", [P, 2, HM, D], F32)

        s_const, s_ctx, s_wqo = sem("s_const"), sem("s_ctx"), sem("s_wqo")
        s_x = sems("s_xin", NCH)
        s_cpool = sem("s_cpool")
        s_mask = sem("s_mask")
        s_setup = sem("s_setup")
        s_zero = sem("s_zero")
        s_tanh = sem("s_tanh")
        s_dve = sem("s_dve")
        s_kh = sem("s_kh")
        s_kl = sem("s_kl")
        s_kout = sem("s_kout")
        s_kin = sem("s_kin")
        s_v = sem("s_v")
        s_ve, s_rstd, s_xn, s_xb = sem("s_ve"), sem("s_rstd"), sem("s_xn"), sem("s_xb")
        s_xt, s_xtl = sem("s_xt"), sem("s_xtl")
        s_qh, s_ql, s_qout, s_qin = sem("s_qh"), sem("s_ql"), sem("s_qout"), sem("s_qin")
        s_mp, s_m0, s_mrep = sem("s_mp"), sem("s_m0"), sem("s_mrep")
        full = sems("misc_full", 2)
        s_vf, s_pmk = sem("s_vf"), sem("s_pmk")
        mx_full, mx_free = sems("mx_full", 2), sems("mx_free", 2)
        sc_full, sc_free = sems("sc_full", 3), sems("sc_free", 3)
        pv_full, pv_free = sem("pv_full"), sem("pv_free")
        s_pl = sem("s_pl")
        s_at, s_att, s_atl = sem("s_at"), sem("s_att"), sem("s_atl")
        s_x2, s_xs = sem("s_x2"), sem("s_xs")
        s_x2out, s_dump = sem("s_x2out"), sem("s_dump")
        s_ve2, s_rstd2 = sem("s_ve2"), sem("s_rstd2")
        s_x2t, s_x2l = sem("s_x2t"), sem("s_x2l")
        s_lg, s_m12, s_gd, s_gx, s_dst = sem("s_lg"), sem("s_m12"), sem("s_gd"), sem("s_gx"), sem("s_dst")
        s_ids = sem("s_ids")
        s_empty = sem("s_empty")
        s_disp = sem("s_disp")
        s_w = sems("s_win", 2)
        s_wl = sem("s_wl")
        s_xg = sems("s_xg", 2)
        t_full, t_free = sems("t_full", 2), sems("t_free", 2)
        h_full, h_free = sems("h_full", 4), sems("h_free", 4)
        y_full, y_free = sems("y_full", 2), sems("y_free", 2)
        s_xgt, s_xgl, s_hl, s_mm1, s_mm2 = sem("s_xgt"), sem("s_xgl"), sem("s_hl"), sem("s_mm1"), sem("s_mm2")
        s_wt, s_b1, s_y, s_add = sem("s_wt"), sem("s_b1"), sem("s_y"), sem("s_add")

        turns, order = misc_turns()
        last_use = {name: order[n - 2] if n >= 2 else None for n, name in enumerate(order)}

        def released(name):
            kind, c = name[0], name[1]
            k = name[2] if len(name) > 2 else 0
            return {"k": (s_kl, c + 1), "v": (s_vf, c + 1), "xt": (s_xt, KD * c + k + 1), "q": (s_ql, KD * c + k + 1),
                    "m": (s_m0, c + 1), "at": (s_att, KD * c + k + 1), "wo": (s_x2, 2 * c + k + 1),
                    "x2t": (s_x2t, KD * c + k + 1), "lg": (s_lg, c + 1), "pos": (s_pmk, c + 1)}[kind]

        def bank(name):
            return ps[:, MISC[turns[name][0]], :]

        def wait_full(eng, name):
            b, n = turns[name]
            eng.wait_ge(full[b], n + 1)

        def second_done(eng, it, par):
            u = ST5 * par + ST5 - 1
            eng.wait_ge(y_full[u % 2], it * ST5 + (u // 2 + 1))

        def before(it, par):
            return (it, 0) if par else (it - 1, 1)

        def first(it, par):
            return isinstance(it, int) and it == 0 and par == 0

        def constants(eng):
            eng.wait_ge(s_const, 16 * 5)

        def late_constants(eng):
            eng.wait_ge(s_cpool, 16 * 5)

        block = ctx.enter_context(nc.Block())
        def view(name, base, shape, dt, at=0):
            t = base[:]
            n = len(t.shape)
            if n == 3:
                t = t.rearrange("p a b -> p (a b)")
            elif n == 4:
                t = t.rearrange("p a b c -> p (a b c)")
            t = t.bitcast(dt)
            size = int(np.prod(shape[1:]))
            assert at + size <= t.shape[1], (name, size, t.shape)
            t = t[0:shape[0], at:at + size]
            if len(shape) == 3:
                t = t.rearrange("p (a b) -> p a b", a=shape[1])
            elif len(shape) == 4:
                t = t.rearrange("p (a b c) -> p a b c", a=shape[1], b=shape[2])
            return t

        w1l = view("w1l", qs, [P, 2, KD, HID], BF16)
        w2l = view("w2l", qs, [P, 2, HM, D], BF16, 2 * KD * HID)
        xg = view("xg", mti, [SLOT, 2, ST5, XW], F32)
        xgt = view("xgt", ks, [P, KD, CAP], F32)
        xgl = view("xgl", ks, [P, KD, CAP], BF16, 2 * KD * CAP)
        wt = sb("wt", [SLOT, ST5], F32)
        hbuf = view("hbuf", x, [P, 7, CAP], F32)
        hb7 = sb("hb7", [P, CAP], F32)
        hl = view("hl", p32, [P, HM, CAP], BF16)
        yb = view("yb", ou, [SLOT, ST5, D], F32)

        def hrow(m):
            return hbuf[:, m, :] if m < 7 else hb7[:, :]

        def load_weights(q, par, e):
            q.dma_start(w1[:, par], a["W1"][bass.ds(e * D, D), :].rearrange("(k p) h -> p k h", p=P)).then_inc(s_w[par], 16)
            q.dma_start(w2[:, par], a["W2"][bass.ds(e * HID, HID), :].rearrange("(m p) d -> p m d", p=P)).then_inc(s_w[par], 16)

        @block.sync
        def _(sp):
            def load_x(c):
                sp.dma_start(x[:, c * QT:(c + 1) * QT, :],
                             a["x"][c * QC:(c + 1) * QC, :].rearrange("(t p) d -> p t d", p=P)).then_inc(s_x[c], 16)

            load_x(0)
            sp.dma_start(idf[:], a["ident"]).then_inc(s_const, 16)
            sp.dma_start(trif[:], a["before"]).then_inc(s_const, 16)
            sp.dma_start(small[:], a["small"]).then_inc(s_const, 16)
            sp.dma_start(bvB[:], bcast(a["bv"], P)).then_inc(s_const, 16)
            sp.dma_start(boB[:], bcast(a["bo"], P)).then_inc(s_const, 16)
            sp.dma_start(wk[:], a["WkT"].rearrange("(k p) n -> p k n", p=P)).then_inc(s_ctx, 16)
            sp.dma_start(ctxT[:], a["ctxT"].rearrange("(k p) b n -> p k b n", p=P)).then_inc(s_ctx, 16)
            sp.dma_start(wv[:], a["WvT"].rearrange("(k p) n -> p k n", p=P)).then_inc(s_ctx, 16)
            for c in range(NCH):
                if c >= 1:
                    load_x(c)
                if c == 0:
                    sp.dma_start(wq[:], a["WqT"].rearrange("(k p) n -> p k n", p=P)).then_inc(s_wqo, 16)
                    sp.dma_start(mqi[:], a["mask"].rearrange("(t p) k -> p t k", p=P)).then_inc(s_mask, 16)
                    sp.dma_start(mti[0:ROWS], a["maskT"].rearrange("(t p) q -> p t q", p=ROWS)).then_inc(s_mask, 16)
                    sp.dma_start(wo[:], a["WoT"].rearrange("(k p) n -> p k n", p=P)).then_inc(s_wqo, 16)
            sp.wait_ge(s_kl, 2)
            for hl_ in range(2):
                sp.dma_start(kq[hl_].rearrange("(k p) n -> p k n", p=P), khl[:, hl_]).then_inc(s_kout, 16)
            sp.wait_ge(s_kout, 32)
            sp.wait_ge(s_zero, 1)
            for g in range(3):
                src = kq[1 if g == 2 else 0]
                for par in range(2):
                    for b in range(B):
                        v = src[:, b * KEYS:(b + 1) * KEYS].rearrange("(j r) n -> r j n", r=2 * DK)
                        sp.dma_start(ks[g * 32 + par * DK:g * 32 + (par + 1) * DK, b, :, par * KEYS:(par + 1) * KEYS],
                                     v[par * DK:(par + 1) * DK]).then_inc(s_kin, 16)
            for b in range(B):
                sp.dma_start(ks[96:128, b, :, 0:PK], a["shift_sel"].bitcast(BF16)).then_inc(s_kin, 16)

            def q_bounce(c):
                sp.wait_ge(s_ql, 2 * (c + 1))
                for h in range(2):
                    sp.dma_start(qd[h][:, c * QC:(c + 1) * QC].rearrange("(k p) n -> p k n", p=P),
                                 qhl[:, h]).then_inc(s_qout, 16)
                sp.wait_ge(s_qout, 32 * (c + 1))
                if c >= 2:
                    sp.wait_ge(sc_full[2], (c - 1) * PAIRS)
                for g in range(3):
                    sp.dma_start(qs[g * 32:(g + 1) * 32, c % 2],
                                 qd[1 if g == 1 else 0][:, c * QC:(c + 1) * QC].rearrange("(j r) n -> r j n", r=32)
                                 ).then_inc(s_qin, 16)

            def m_spread(c):
                sp.wait_ge(s_m0, c + 1)
                one = qs[96:128, c % 2, 0:1, :]
                sp.dma_start(qs[96:128, c % 2, 1:PAIRS, :], one.to_broadcast([32, PAIRS - 1, QC])).then_inc(s_mrep, 16)

            def x2_out(c):
                sp.wait_ge(s_x2, 2 * (c + 1))
                sp.dma_start(a["out"][c * QC:(c + 1) * QC, :].rearrange("(t p) d -> p t d", p=P),
                             x2[:]).then_inc(s_x2out, 16)

            q_bounce(0)
            m_spread(0)
            for c in range(NCH):
                if c + 1 < NCH:
                    q_bounce(c + 1)
                if c >= 1:
                    x2_out(c - 1)
                if c + 1 < NCH:
                    m_spread(c + 1)
            x2_out(NCH - 1)

            def load_rows(e, par):
                sp.dma_start(xg[:, par, 0:4, :],
                             rows[bass.ds(e * CAP, 4 * SLOT), :].rearrange("(t p) c -> p t c", p=SLOT)
                             ).then_inc(s_xg[par], 16)
                sp.dma_start(xg[0:LAST, par, 4, :], rows[bass.ds(e * CAP + 4 * SLOT, LAST), :]).then_inc(s_xg[par], 16)

            sp.wait_ge(s_disp, 16 * 2 * NT)
            for par in range(2):
                load_rows(par, par)

            def next_loads(it, par):
                e = it * 2 + par
                second_done(sp, it, par)
                load_weights(sp, par, e + 2)
                sp.wait_ge(s_add, (e + 1) * (16 * ST5))
                load_rows(e + 2, par)

            with sp.Fori(0, E // 2 - 1) as it:
                next_loads(it, 0)
                next_loads(it, 1)
            sp.wait_ge(s_add, 16 * ST5 * E)

        @block.gpsimd
        def _(pool):
            pool.dma_start(b1T[:], a["b1T"]).then_inc(s_cpool, 16)
            pool.dma_start(b2B[:], bcast(a["b2"], P)).then_inc(s_cpool, 16)
            pool.dma_start(tokid[:], a["tokid"]).then_inc(s_cpool, 16)
            pool.dma_start(dumpf[:], a["dump"]).then_inc(s_cpool, 16)
            pool.dma_start(wgf[:], a["Wg"].rearrange("(k p) e -> p k e", p=P)).then_inc(s_cpool, 16)
            pool.memset(ks[:].rearrange("p b j k -> p (b j k)").bitcast(U32), 0).then_inc(s_zero, 1)
            pool.memset(mp[:].rearrange("p a b -> p (a b)").bitcast(U32), 0).then_inc(s_zero, 1)
            pool.memset(vs[:].rearrange("p b t j v -> p (b t j v)").bitcast(U32), 0).then_inc(s_zero, 1)
            pool.memset(carry[:].bitcast(U32), 0).then_inc(s_zero, 1)
            constants(pool)

            def rsqrt(c, src, out, ready, done):
                pool.wait_ge(ready, c + 1)
                pool.tensor_tensor(out[:], src[:], half, ALU.pow).then_inc(done, 1)

            def add_bias(c):
                pool.wait_ge(s_xn, QT * (c + 1))
                if c == 0:
                    pool.wait_ge(s_setup, 1)
                for i in range(QT):
                    pool.tensor_tensor(x[:, c * QT + i, :], x[:, c * QT + i, :], boB[:], ALU.add).then_inc(s_xb, 1)

            def ids(c):
                if c >= 2:
                    pool.wait_ge(s_disp, 16 * 2 * QT * (c - 1))
                v = xs[:, c % 2, :, D:D + 1].bitcast(I32)
                pool.tensor_copy(v, tokid[:, c * QT:(c + 1) * QT].unsqueeze(2)).then_inc(s_ids, 1)

            def dispatch(c, tiles):
                if tiles[0] == 0:
                    pool.wait_ge(s_dst, c + 1)
                    if c == 0:
                        pool.wait_ge(s_empty, 16 * E)
                    pool.wait_ge(s_ids, c + 1)
                for i in tiles:
                    for k in range(2):
                        t = c * QT + i
                        pool.indirect_dma_start(
                            out=rows, out_offset=bass.IndirectOffsetOnAxis(ap=dsti[:, k, t:t + 1].bitcast(U32), axis=0),
                            in_=xs[:, c % 2, i, :], in_offset=None).then_inc(s_disp, 16)

            rsqrt(0, ve, rstd, s_ve, s_rstd)
            late_constants(pool)
            rsqrt(1, ve, rstd, s_ve, s_rstd)
            ids(0)
            ids(1)
            add_bias(0)
            add_bias(1)
            for c in range(NCH):
                if c >= 1:
                    rsqrt(c - 1, ve2, rstd2, s_ve2, s_rstd2)
                if c < 2:
                    for i in range(E // 2):
                        e = c * (E // 2) + i
                        pool.wait_ge(sc_full[2], c * PAIRS + i + 4)
                        pool.dma_start(rows[e * CAP:(e + 1) * CAP, :], a["empty"]).then_inc(s_empty, 16)
                if c == 1:
                    pool.dma_start(a["out"][TOK:TOK + CAP, :], a["empty"][:, 0:D]).then_inc(s_dump, 16)
                if c >= 1:
                    dispatch(c - 1, range(1))
                if c + 2 < NCH:
                    rsqrt(c + 2, ve, rstd, s_ve, s_rstd)
                if c >= 1:
                    dispatch(c - 1, range(1, QT))
                    if c + 1 < NCH:
                        ids(c + 1)
                if c + 2 < NCH:
                    add_bias(c + 2)
            rsqrt(NCH - 1, ve2, rstd2, s_ve2, s_rstd2)
            dispatch(NCH - 1, range(QT))

            pool.wait_ge(s_x2out, 16 * NCH)
            pool.wait_ge(s_dump, 16)
            for e in range(E):
                if e >= 1:
                    pool.wait_ge(s_add, e * 16 * ST5)
                for t in range(ST5):
                    n = SLOT if t < 4 else LAST
                    pool.wait_ge(s_y, e * ST5 + t + 1)
                    pool.indirect_dma_start(
                        out=a["out"], out_offset=bass.IndirectOffsetOnAxis(
                            ap=xg[0:n, e % 2, t, D:D + 1].bitcast(U32), axis=0),
                        in_=yb[0:n, t, :], in_offset=None, compute_op=ALU.add).then_inc(s_add, 16)

        @block.scalar
        def _(act):
            def q_high(c):
                for f in range(KD):
                    wait_full(act, ("q", c, f))
                    if f == 0 and c >= 1:
                        act.wait_ge(s_qout, 32 * c)
                    act.activation(qhl[:, 0, f, :], bank(("q", c, f)), ACT.Identity,
                                   bias=bq[:, f:f + 1]).then_inc(s_qh, 1)

            def turn(name, out, done, c, readers=()):
                for k in range(KD):
                    wait_full(act, (name, c, k))
                    if k == 0:
                        for s, v in readers:
                            act.wait_ge(s, v)
                    act.activation(out[:, k, :], bank((name, c, k)), ACT.Copy).then_inc(done, 1)

            def m_rows(c):
                wait_full(act, ("m", c))
                if c >= 2:
                    act.wait_ge(sc_full[2], (c - 1) * PAIRS)
                act.activation(qs[96:128, c % 2, 0, :], bank(("m", c)).bitcast(BF16)[96:128, 0:QC],
                               ACT.Copy).then_inc(s_m0, 1)

            def logits(c):
                wait_full(act, ("lg", c))
                if c >= 1:
                    act.wait_ge(s_gd, c)
                act.activation(lg16[:].rearrange("p t e -> p (t e)"), bank(("lg", c))[:, 0:QT * 2 * E],
                               ACT.Copy).then_inc(s_lg, 1)

            def gate_exp(c):
                act.wait_ge(s_gd, c + 1)
                act.activation(gx[:], gd[:], ACT.Exp).then_inc(s_gx, 1)

            def exps(c, j):
                n = c * PAIRS + j
                for t in range(3):
                    act.wait_ge(sc_full[t], n + 1)
                    if t == 0 and n >= 2:
                        act.wait_ge(pv_full, n - 1)
                    act.activation(p32[0:ROWS, n % 2, t, :], ps[0:ROWS, SC[t], :], ACT.Exp,
                                   scale=float(DK) ** -0.5).then_inc(sc_free[t], 1)

            def pv_out(c, j):
                n = c * PAIRS + j
                act.wait_ge(pv_full, n + 1)
                if j == 0 and c >= 1:
                    act.wait_ge(s_at, c)
                v = ou[:].rearrange("p (i j) v -> p i j v", i=QT)[:, :, j, :]
                act.activation(v, ps[:, PVB, 0:QT * VW].rearrange("p (i v) -> p i v", i=QT),
                               ACT.Copy).then_inc(pv_free, 1)

            def post(c, j):
                if j == 1:
                    turn("at", att, s_att, c, [(s_lg, c)] if c else ())
                if j == 4:
                    turn("x2t", x2t, s_x2t, c, [(s_x2, 2 * (c + 1))])
                if j == 5:
                    logits(c)
                if j == 7:
                    gate_exp(c)

            constants(act)
            act.activation(small[:, 6:8], small[:, 4:6], ACT.Tanh).then_inc(s_tanh, 1)
            for f in range(KD):
                wait_full(act, ("k", f))
                act.activation(khl[:, 0, f, :], bank(("k", f))[:, 0:2 * KEYS], ACT.Identity,
                               bias=bk[:, f:f + 1]).then_inc(s_kh, 1)
            turn("xt", xt, s_xt, 0)
            q_high(0)
            m_rows(0)
            for c in range(NCH):
                for j in range(PAIRS):
                    exps(c, j)
                    if c < 2 and j == 5:
                        load_weights(act, c, c)
                    if c + 1 < NCH:
                        if j == 0:
                            turn("xt", xt, s_xt, c + 1, [(s_ql, 2 * (c + 1))])
                        if j == 1:
                            q_high(c + 1)
                    if c >= 1:
                        post(c - 1, j)
                    if j == 7 and c + 1 < NCH:
                        m_rows(c + 1)
                    if j >= 1:
                        pv_out(c, j - 1)
                pv_out(c, PAIRS - 1)
            for j in range(PAIRS):
                post(NCH - 1, j)

            def t_parts(it, par, k):
                u = 3 * par + k
                return u % 2, it * 3 + u // 2

            def turn_rows(it, par):
                e = it * 2 + par
                if not first(it, par):
                    act.wait_ge(h_full[3], e * 4)
                for k in range(3):
                    b, n = t_parts(it, par, k)
                    act.wait_ge(t_full[b], n + 1)
                    if k < 2:
                        o, i = xgt[:, k, 0:4 * SLOT], ps[:, T_BANK[b], 0:4 * SLOT]
                    else:
                        o = xgt[:, :, 4 * SLOT:CAP]
                        i = ps[:, T_BANK[b], 0:2 * LAST].rearrange("p (k n) -> p k n", k=KD)
                    act.activation(o, i, ACT.Copy).then_inc(t_free[b], 1)

            def gelus(it, par):
                e = it * 2 + par
                act.activation(b1c[:, par, :], b1T[:, bass.ds(e * HM, HM)], ACT.Copy).then_inc(s_b1, 1)
                act.wait_ge(s_b1, e + 1)
                for m in range(HM):
                    for ch in range(2):
                        b = (2 * m + ch) % 4
                        act.wait_ge(h_full[b], e * 4 + (m // 2 + 1))
                        if m == 0 and ch == 0 and not first(it, par):
                            second_done(act, *before(it, par))
                        w = slice(0, CA) if ch == 0 else slice(CA, CAP)
                        act.activation(hrow(m)[:, w], ps[:, H_BANK[b], 0:(CA if ch == 0 else CB)],
                                       ACT.Gelu_apprx_tanh, bias=b1c[:, par, m:m + 1]).then_inc(h_free[b], 1)

            def expert(it, par, last=False):
                gelus(it, par)
                if not last:
                    if par == 0:
                        turn_rows(it, 1)
                    else:
                        turn_rows(it + 1, 0)

            late_constants(act)
            turn_rows(0, 0)
            expert(0, 0)
            expert(0, 1)
            with act.Fori(1, E // 2 - 1) as it:
                expert(it, 0)
                expert(it, 1)
            expert(E // 2 - 1, 0)
            expert(E // 2 - 1, 1, last=True)

        @block.vector
        def _(dve):
            own = [0]

            def link(ins):
                own[0] += 1
                ins.then_inc(s_dve, 1)
                dve.wait_ge(s_dve, own[0])

            def mark(ins):
                own[0] += 1
                ins.then_inc(s_dve, 1)

            def settle():
                dve.wait_ge(s_dve, own[0])

            def lown(eng_out, full_):
                return dve.tensor_tensor(eng_out, full_, hi(full_), ALU.subtract)

            def norm(c, src, st, mvt, vet, rs, out, s_v_, s_r, s_out):
                for i in range(QT):
                    mark(dve.bn_stats(st[:, i, :], src(i)))
                settle()
                for i in range(QT):
                    mark(dve.bn_aggr(mvt[:, i, :], st[:, i, :]))
                settle()
                dve.tensor_scalar(vet[:].unsqueeze(2), mvt[:, :, 1:2], EPS, None, ALU.add).then_inc(s_v_, 1)
                dve.wait_ge(s_r, c + 1)
                for i in range(QT):
                    dve.tensor_scalar(out(i), src(i), mvt[:, i, 0:1], rs[:, i:i + 1], ALU.subtract,
                                      ALU.mult).then_inc(s_out, 1)

            def norm_x(c):
                dve.wait_ge(s_x[c], 16)
                if c >= 1:
                    dve.wait_ge(full[turns[("xt", c - 1, 1)][0]], turns[("xt", c - 1, 1)][1] + 1)
                norm(c, lambda i: x[:, c * QT + i, :], st6, mv, ve, rstd, lambda i: xn[:, i, :], s_ve, s_rstd, s_xn)

            def low_xt(c):
                dve.wait_ge(s_xt, 2 * (c + 1))
                lown(xtl[:], xt[:]).then_inc(s_xtl, 1)

            def q_low(c):
                for f in range(KD):
                    dve.wait_ge(s_qh, 2 * c + f + 1)
                    dve.scalar_tensor_tensor(out=qhl[:, 1, f, :], in0=bank(("q", c, f)), scalar=bq[:, f:f + 1],
                                             in1=qhl[:, 0, f, :], op0=ALU.add, op1=ALU.subtract).then_inc(s_ql, 1)

            def maxes(c, js):
                for j in js:
                    for i in range(QT):
                        n = (c * PAIRS + j) * QT + i
                        dve.wait_ge(mx_full[n % 2], n // 2 + 1)
                        dve.tensor_reduce(nm[:, i, 2 * j:2 * j + 2],
                                          ps[:, MX[n % 2], 0:2 * KEYS].rearrange("p (h k) -> p h k", h=2),
                                          AX.X, ALU.max, negate=True).then_inc(mx_free[n % 2], 1)

            def m_halves(c):
                dve.wait_ge(mx_free[0], (c + 1) * PAIRS * QT // 2)
                dve.wait_ge(mx_free[1], (c + 1) * PAIRS * QT // 2)
                if c == 0:
                    dve.wait_ge(s_zero, 2)
                else:
                    dve.wait_ge(s_m0, c)
                link(dve.tensor_copy(mp[:, :, 96:112], nm[:]))
                dve.tensor_tensor(mp[:, :, 112:128], nm[:], mp[:, :, 96:112], ALU.subtract).then_inc(s_mp, 1)

            def lows(c, j):
                n = c * PAIRS + j
                for t in range(3):
                    dve.wait_ge(sc_free[t], n + 1)
                lown(pl[:, n % 2], p32[0:ROWS, n % 2]).then_inc(s_pl, 1)

            def attend(c):
                dve.wait_ge(pv_free, (c + 1) * PAIRS)
                if c >= 1:
                    dve.wait_ge(full[turns[("at", c - 1, 1)][0]], turns[("at", c - 1, 1)][1] + 1)
                mark(dve.reciprocal(rd[:], ou[:, :, 64:66]))
                v = ou[:, :, 0:64].rearrange("p n (h l d) -> p n h l d", h=2, l=2)
                for h in range(2):
                    mark(dve.tensor_tensor(at[:, :, h, :], v[:, :, h, 0, :], v[:, :, h, 1, :], ALU.add))
                settle()
                dve.tensor_tensor(at[:], at[:], rd[:].unsqueeze(3).to_broadcast([P, QT * PAIRS, 2, DK]),
                                  ALU.mult).then_inc(s_at, 1)

            def low_att(c):
                dve.wait_ge(s_att, 2 * (c + 1))
                lown(atl[:], att[:]).then_inc(s_atl, 1)

            def residual(c):
                for g in range(2):
                    wait_full(dve, ("wo", c, g))
                    if g == 0:
                        dve.wait_ge(s_xb, QT * (c + 1))
                        if c >= 1:
                            dve.wait_ge(s_x2out, 16 * c)
                    t = c * QT + 2 * g
                    o = dve.scalar_tensor_tensor(
                        out=x2[:, 2 * g:2 * g + 2, :].rearrange("p t d -> p (t d)"), in0=bank(("wo", c, g)), scalar=tgx,
                        in1=x[:, t:t + 2, :].rearrange("p t d -> p (t d)"), op0=ALU.mult, op1=ALU.add)
                    o.then_inc(s_x2, 1)

            def norm_x2(c):
                dve.wait_ge(s_x2, 2 * (c + 1))
                if c >= 2:
                    dve.wait_ge(s_disp, 16 * 2 * QT * (c - 1))
                norm(c, lambda i: x2[:, i, :], st62, mv2, ve2, rstd2, lambda i: xs[:, c % 2, i, 0:D],
                     s_ve2, s_rstd2, s_xs)

            def low_x2(c):
                dve.wait_ge(s_x2t, 2 * (c + 1))
                lown(x2l[:], x2t[:]).then_inc(s_x2l, 1)

            def choose(c):
                dve.wait_ge(s_lg, c + 1)
                link(dve.tensor_tensor(lg[:], lg16[:, :, 0:E], lg16[:, :, E:2 * E], ALU.add))
                src = lg
                for k in range(2):
                    link(dve.tensor_reduce(l12[:, k, :], src[:], AX.X, ALU.max))
                    link(dve.tensor_tensor(eqs[:], src[:], l12[:, k, :].unsqueeze(2).to_broadcast([P, QT, E]), ALU.is_equal))
                    link(dve.tensor_tensor(eqs[:], eqs[:], rank.unsqueeze(1).to_broadcast([P, QT, E]), ALU.mult))
                    link(dve.tensor_reduce(s12[:, k, :], eqs[:], AX.X, ALU.max))
                    link(dve.tensor_tensor(m12[:, k], eqs[:], s12[:, k, :].unsqueeze(2).to_broadcast([P, QT, E]), ALU.is_equal))
                    if k == 0:
                        link(dve.scalar_tensor_tensor(out=lgb[:], in0=m12[:, 0], scalar=-1e30, in1=lg[:],
                                                      op0=ALU.mult, op1=ALU.add))
                        src = lgb
                dve.tensor_tensor(gd[:], l12[:, 1, :], l12[:, 0, :], ALU.subtract).then_inc(s_gd, 1)
                link(dve.tensor_tensor(msum[:], m12[:, 0], m12[:, 1], ALU.add))
                if c == 0:
                    dve.wait_ge(s_zero, 4)
                link(dve.tensor_copy(mcum[:, 0, :], carry[:]))
                for i in range(1, QT):
                    link(dve.tensor_tensor(mcum[:, i, :], mcum[:, i - 1, :], msum[:, i - 1, :], ALU.add))
                dve.tensor_tensor(carry[:], mcum[:, QT - 1, :], msum[:, QT - 1, :], ALU.add).then_inc(s_m12, 1)

            def place(c):
                wait_full(dve, ("pos", c))
                pos = bank(("pos", c))[:, 0:QT * E].unsqueeze(1).to_broadcast([P, 2, QT * E])
                dve.tensor_tensor(pmk[:].rearrange("p k t e -> p k (t e)"), pos,
                                  m12[:].rearrange("p k t e -> p k (t e)"), ALU.mult).then_inc(s_pmk, 1)
                dve.wait_ge(s_pmk, c + 1)
                link(dve.tensor_reduce(posk[:], pmk[:], AX.X, ALU.add))
                mark(dve.tensor_scalar(keep[:], posk[:], float(CAP), None, ALU.is_lt))
                link(dve.tensor_scalar(dst[:], s12[:], -float(CAP), float(E * CAP), ALU.mult, ALU.add))
                link(dve.tensor_tensor(dst[:], dst[:], posk[:], ALU.add))
                dump = dumpf[:, :, c * QT:(c + 1) * QT]
                link(dve.tensor_tensor(dst[:], dst[:], dump, ALU.subtract))
                link(dve.tensor_tensor(dst[:], dst[:], keep[:], ALU.mult))
                mark(dve.tensor_tensor(dsti[:, :, c * QT:(c + 1) * QT], dst[:], dump, ALU.add))
                dve.wait_ge(s_gx, c + 1)
                w = xs[:, c % 2]
                link(dve.tensor_scalar(gr[:], gx[:], 1.0, None, ALU.add))
                link(dve.reciprocal(gr[:], gr[:]))
                link(dve.tensor_scalar(gr[:], gr[:], tgf, None, ALU.mult))
                link(dve.tensor_tensor(w[:, :, D + 1], gr[:], gx[:], ALU.mult))
                mark(dve.tensor_tensor(w[:, :, D + 2], gr[:], w[:, :, D + 1], ALU.subtract))
                settle()
                dve.tensor_copy(w[:, :, D + 3], s12[:, 0, :]).then_inc(s_dst, 1)

            def post(c, j):
                if j == 0:
                    attend(c)
                if j == 1:
                    low_att(c)
                if j == 2:
                    residual(c)
                    norm_x2(c)
                if j == 4:
                    low_x2(c)
                if j == 6:
                    choose(c)
                if j == 7:
                    place(c)

            def own_values(b):
                for t in range(3):
                    i = 3 * b + t
                    settle()
                    wait_full(dve, ("v", i))
                    dve.tensor_tensor(vf[:], bank(("v", i))[0:ROWS, 0:D], bvB[0:ROWS, :],
                                      ALU.add).then_inc(s_vf, 1)
                    dve.wait_ge(s_vf, i + 1)
                    for h in range(2):
                        mine = small[0:ROWS, 16 + 3 * h + t:17 + 3 * h + t]
                        v = vf[:].rearrange("p (j h d) -> p j h d", h=2, d=DK)[:, :, h, :]
                        o = vs[:, b, t, :, 32 * h:32 * h + 32].rearrange("p j (l d) -> p j l d", l=2)
                        link(dve.tensor_scalar(o[:, :, 0, :], v, mine, None, ALU.mult))
                        mark(dve.scalar_tensor_tensor(out=o[:, :, 1, :], in0=v, scalar=mine, in1=o[:, :, 0, :],
                                                      op0=ALU.mult, op1=ALU.subtract))
                        dve.tensor_copy(vs[:, b, t, :, 64 + h], mine.to_broadcast([ROWS, PAIRS])).then_inc(s_v, 1)

            def low_weights():
                mark(lown(wol[:], wo[:]))
                for k in range(KD):
                    link(dve.tensor_copy(wg16[:, k, 0:E], wgf[:, k, :]))
                    mark(dve.tensor_tensor(wg16[:, k, E:2 * E], wgf[:, k, :], wg16[:, k, 0:E], ALU.subtract))

            norm_x(0)
            constants(dve)
            dve.wait_ge(s_tanh, 1)
            mark(dve.tensor_copy(idb[:], idf[:]))
            mark(dve.tensor_copy(trib[:], trif[:]))
            mark(dve.memset(onesb[:], 1.0))
            dve.tensor_scalar(boB[:], boB[:], tgx, None, ALU.mult).then_inc(s_setup, 1)
            settle()
            for f in range(KD):
                dve.wait_ge(s_kh, f + 1)
                dve.scalar_tensor_tensor(out=khl[:, 1, f, :], in0=bank(("k", f))[:, 0:2 * KEYS], scalar=bk[:, f:f + 1],
                                         in1=khl[:, 0, f, :], op0=ALU.add, op1=ALU.subtract).then_inc(s_kl, 1)
            dve.wait_ge(s_wqo, 32)
            mark(lown(wql[:], wq[:]))
            low_xt(0)
            dve.wait_ge(s_mask, 32)
            mark(dve.tensor_scalar(mq[:], mqi[:], 0, -BIG, ALU.is_equal, ALU.mult))
            dve.tensor_scalar(mt[:], mti[0:ROWS], 0, -BIG, ALU.is_equal, ALU.mult).then_inc(s_setup, 1)
            q_low(0)
            norm_x(1)
            late_constants(dve)
            dve.wait_ge(s_zero, 3)
            own_values(0)
            maxes(0, range(PAIRS))
            m_halves(0)
            for c in range(NCH):
                for j in range(PAIRS):
                    if c + 1 < NCH:
                        if j == 0:
                            low_xt(c + 1)
                        if j == 1:
                            q_low(c + 1)
                        if 3 <= j <= 6:
                            maxes(c + 1, (2 * j - 6, 2 * j - 5))
                    if j == 7 and c + 1 < NCH:
                        m_halves(c + 1)
                    if c == 0 and j == 2:
                        own_values(1)
                        low_weights()
                    late = j in (2, 6, 7)
                    if late:
                        lows(c, j)
                    if c >= 1:
                        post(c - 1, j)
                    if not late:
                        lows(c, j)
                if c + 2 < NCH:
                    norm_x(c + 2)
            for j in range(PAIRS):
                post(NCH - 1, j)

            def weight_part(par, g):
                k, h = g // 4, (g % 4) * (HID // 4)
                lown(w1l[:, par, k, h:h + HID // 4], w1[:, par, k, h:h + HID // 4]).then_inc(s_wl, 1)
                lown(w2l[:, par, g, :], w2[:, par, g, :]).then_inc(s_wl, 1)

            def low_rows(it, par):
                e = it * 2 + par
                for k in range(3):
                    u = 3 * par + k
                    dve.wait_ge(t_free[u % 2], it * 3 + (u // 2 + 1))
                lown(xgl[:], xgt[:]).then_inc(s_xgl, 1)

            def low_hidden(it, par, m):
                e = it * 2 + par
                for ch in range(2):
                    dve.wait_ge(h_free[(2 * m + ch) % 4], e * 4 + (m // 2 + 1))
                lown(hl[:, m, :], hrow(m)).then_inc(s_hl, 1)

            def row_weights(it, par):
                e = it * 2 + par
                dve.wait_ge(s_xg[par], it * 32 + 32)
                if not (isinstance(e, int) and e == 0):
                    dve.wait_ge(s_y, e * ST5)
                for n, t0, t1 in ((SLOT, 0, 4), (LAST, 4, 5)):
                    dve.tensor_tensor(wt[0:n, t0:t1], xg[0:n, par, t0:t1, D + 3],
                                      rank[0:n, bass.ds(e, 1)].to_broadcast([n, t1 - t0]), ALU.is_equal).then_inc(s_wt, 1)
                dve.wait_ge(s_wt, e * 6 + 2)
                for n, t0, t1 in ((SLOT, 0, 4), (LAST, 4, 5)):
                    dve.tensor_tensor(wt[0:n, t0:t1], wt[0:n, t0:t1], xg[0:n, par, t0:t1, D + 2],
                                      ALU.mult).then_inc(s_wt, 1)
                dve.wait_ge(s_wt, e * 6 + 4)
                for n, t0, t1 in ((SLOT, 0, 4), (LAST, 4, 5)):
                    dve.tensor_tensor(wt[0:n, t0:t1], wt[0:n, t0:t1], xg[0:n, par, t0:t1, D + 1],
                                      ALU.add).then_inc(s_wt, 1)
                dve.wait_ge(s_wt, e * 6 + 6)

            def outputs(it, par, last):
                e = it * 2 + par
                for t in range(ST5):
                    if t < 4 and not last:
                        weight_part(1 - par, 2 * t)
                        weight_part(1 - par, 2 * t + 1)
                    n = SLOT if t < 4 else LAST
                    u = ST5 * par + t
                    dve.wait_ge(y_full[u % 2], it * 5 + (u // 2 + 1))
                    if t == 0 and not (isinstance(e, int) and e == 0):
                        dve.wait_ge(s_add, e * (16 * ST5))
                    dve.tensor_tensor(yb[0:n, t, :], ps[0:n, Y_BANK[u % 2], 0:D], b2B[0:n, bass.ds(e * D, D)],
                                      ALU.add).then_inc(y_free[u % 2], 1)
                    dve.wait_ge(y_free[u % 2], it * 5 + (u // 2 + 1))
                    dve.tensor_scalar(yb[0:n, t, :], yb[0:n, t, :], wt[0:n, t:t + 1], None, ALU.mult).then_inc(s_y, 1)

            def expert(it, par, last=False):
                if not last:
                    o = 1 - par
                    dve.wait_ge(s_w[o], (it + par) * 32 + 32)
                    if not first(it, par):
                        second_done(dve, *before(it, par))
                for m in range(HM):
                    low_hidden(it, par, m)
                row_weights(it, par)
                if not last:
                    low_rows(it + par, 1 - par)
                outputs(it, par, last)

            dve.wait_ge(s_w[0], 32)
            for g in range(8):
                weight_part(0, g)
            low_rows(0, 0)
            expert(0, 0)
            expert(0, 1)
            with dve.Fori(1, E // 2 - 1) as it:
                expert(it, 0)
                expert(it, 1)
            expert(E // 2 - 1, 0)
            expert(E // 2 - 1, 1, last=True)

        @block.tensor
        def _(pe):
            def begin(name):
                if last_use[name]:
                    pe.wait_ge(*released(last_use[name]))
                return bank(name)

            def finish(name, mm):
                mm.then_inc(full[turns[name][0]], 1)

            def transposes(name, c, src):
                for k in range(KD):
                    o = begin((name, c, k))
                    for i in range(QT):
                        mm = pe.transpose(o[:, i * P:(i + 1) * P], src(i, k), idf[:])
                    finish((name, c, k), mm)

            def product3(out, lhs, rhs, parts):
                n = 0
                for k in range(parts):
                    lh, ll = lhs(k)
                    rh, rl = rhs(k)
                    for l, r in ((lh, rh), (lh, rl), (ll, rh)):
                        mm = pe.matmul(out, l, r, start=(n == 0), stop=(n == 3 * parts - 1))
                        n += 1
                return mm

            def queries(c):
                pe.wait_ge(s_xtl, c + 1)
                for f in range(KD):
                    o = begin(("q", c, f))
                    w = slice(f * P, (f + 1) * P)
                    mm = product3(o, lambda k: (hi(wq[:, k, w]), wql[:, k, w]),
                                  lambda k: (hi(xt[:, k, :]), xtl[:, k, :]), KD)
                    finish(("q", c, f), mm)

            def score_rows(c, js, tiles=range(QT)):
                b = c // (NCH // B)
                for j in js:
                    for i in tiles:
                        n = (c * PAIRS + j) * QT + i
                        if n >= 2:
                            pe.wait_ge(mx_free[n % 2], n // 2)
                        o = ps[:, MX[n % 2], 0:2 * KEYS]
                        qt = (c * QT + i) % (S // P)
                        pe.matmul(o.rearrange("p (h k) -> p h k", h=2), idb[:],
                                  mq[:, qt:qt + 1, :].to_broadcast([P, 2, KEYS]), start=True, stop=False)
                        pe.matmul(o, qs[0:96, c % 2, j, i * P:(i + 1) * P], ks[0:96, b, j, 0:2 * KEYS],
                                  start=False, stop=True).then_inc(mx_full[n % 2], 1)

            def shift_rows(c):
                pe.wait_ge(s_mp, c + 1)
                o = begin(("m", c)).bitcast(BF16)
                for i in range(QT):
                    mm = pe.transpose(o[:, i * P:(i + 1) * P], mp[:, i, :], idb[:])
                finish(("m", c), mm)

            def scores(c, j):
                n = c * PAIRS + j
                b = c // (NCH // B)
                q0 = (c * QC) % S
                for t in range(3):
                    if n >= 1:
                        pe.wait_ge(sc_free[t], n)
                    o = ps[0:ROWS, SC[t], :]
                    pe.matmul(o, idb[0:ROWS, 0:ROWS], mt[:, t, q0:q0 + QC], start=True, stop=False)
                    pe.matmul(o, ks[:, b, j, t * ROWS:(t + 1) * ROWS], qs[:, c % 2, j, :],
                              start=False, stop=True).then_inc(sc_full[t], 1)

            def values(c, j, tiles=range(QT)):
                n = c * PAIRS + j
                b = c // (NCH // B)
                if tiles[0] == 0:
                    pe.wait_ge(s_pl, n + 1)
                    if n >= 1:
                        pe.wait_ge(pv_free, n)
                for i in tiles:
                    q = slice(i * P, (i + 1) * P)
                    for t in range(3):
                        v = vs[:, b, t, j, :]
                        o = ps[:, PVB, i * VW:(i + 1) * VW]
                        pe.matmul(o, hi(p32[0:ROWS, n % 2, t, q]), v, start=(t == 0), stop=False)
                        mm = pe.matmul(o, pl[:, n % 2, t, q], v, start=False, stop=(t == 2))
                if tiles[-1] == QT - 1:
                    mm.then_inc(pv_full, 1)

            def post(c, j):
                if j == 1:
                    pe.wait_ge(s_at, c + 1)
                    v = at[:].rearrange("p (i j) h d -> p i (j h d)", i=QT)
                    transposes("at", c, lambda i, k: v[:, i, k * P:(k + 1) * P])
                if j == 2:
                    pe.wait_ge(s_atl, c + 1)
                    for g in range(2):
                        o = begin(("wo", c, g))
                        for u in range(2):
                            q = slice((2 * g + u) * P, (2 * g + u + 1) * P)
                            mm = product3(o[:, u * D:(u + 1) * D], lambda k: (hi(att[:, k, q]), atl[:, k, q]),
                                          lambda k: (hi(wo[:, k, :]), wol[:, k, :]), KD)
                        finish(("wo", c, g), mm)
                if j == 4:
                    pe.wait_ge(s_xs, QT * (c + 1))
                    transposes("x2t", c, lambda i, k: xs[:, c % 2, i, k * P:(k + 1) * P])
                if j == 5:
                    pe.wait_ge(s_x2l, c + 1)
                    o = begin(("lg", c))
                    for i in range(QT):
                        q = slice(i * P, (i + 1) * P)
                        for k in range(KD):
                            pe.matmul(o[:, i * 16:(i + 1) * 16], hi(x2t[:, k, q]), wg16[:, k, :],
                                      start=(k == 0), stop=False)
                            mm = pe.matmul(o[:, i * 16:(i + 1) * 16], x2l[:, k, q], wg16[:, k, :],
                                           start=False, stop=(k == KD - 1))
                    finish(("lg", c), mm)
                if j == 7:
                    pe.wait_ge(s_m12, c + 1)
                    o = begin(("pos", c))[:, 0:QT * E]
                    pe.matmul(o, trib[:], msum[:].rearrange("p t e -> p (t e)"), start=True, stop=False)
                    mm = pe.matmul(o, onesb[:], mcum[:].rearrange("p t e -> p (t e)"), start=False, stop=True)
                    finish(("pos", c), mm)

            def own_values(b):
                for t in range(3):
                    i = 3 * b + t
                    o = begin(("v", i))[0:ROWS, 0:D]
                    for k in range(KD):
                        mm = pe.matmul(o, ctxT[:, k, b, t * ROWS:(t + 1) * ROWS], wv[:, k, :], start=(k == 0), stop=(k == KD - 1))
                    finish(("v", i), mm)

            pe.wait_ge(s_ctx, 48)
            for f in range(KD):
                o = begin(("k", f))[:, 0:2 * KEYS].rearrange("p (b k) -> p b k", b=B)
                for k in range(KD):
                    mm = pe.matmul(o, wk[:, k, f * P:(f + 1) * P], ctxT[:, k, :, 0:KEYS], start=(k == 0), stop=(k == KD - 1))
                finish(("k", f), mm)
            constants(pe)
            pe.wait_ge(s_xn, QT)
            transposes("xt", 0, lambda i, k: xn[:, i, k * P:(k + 1) * P])
            queries(0)
            own_values(0)
            pe.wait_ge(s_setup, 2)
            pe.wait_ge(s_qin, 48)
            pe.wait_ge(s_kin, 16 * 14)
            score_rows(0, range(PAIRS))
            shift_rows(0)
            for c in range(NCH):
                for j in range(PAIRS):
                    if j == 0:
                        pe.wait_ge(s_m0, c + 1)
                    if j == 1:
                        pe.wait_ge(s_mrep, 16 * (c + 1))
                    scores(c, j)
                    if c + 1 < NCH:
                        if j == 0:
                            pe.wait_ge(s_xn, QT * (c + 2))
                            transposes("xt", c + 1, lambda i, k: xn[:, i, k * P:(k + 1) * P])
                        if j == 1:
                            queries(c + 1)
                        if j == 3:
                            pe.wait_ge(s_qin, 48 * (c + 2))
                        if 3 <= j <= 6:
                            for g in range(2 * QT):
                                score_rows(c + 1, (2 * j - 6 + g // QT,), (g % QT,))
                                if g % 2:
                                    values(c, j - 1, (g // 2,))
                        if j == 7:
                            shift_rows(c + 1)
                    if c >= 1:
                        post(c - 1, j)
                    if c == 0 and j == 1:
                        pe.wait_ge(s_v, 6)
                    if c == 0 and j == 2:
                        own_values(1)
                    if c == NCH // B and j == 1:
                        pe.wait_ge(s_v, 12)
                    if j >= 1 and not (c + 1 < NCH and 3 <= j <= 6):
                        values(c, j - 1)
                values(c, PAIRS - 1)
            for j in range(PAIRS):
                post(NCH - 1, j)

            def turn_rows(it, par):
                pe.wait_ge(s_xg[par], it * 32 + 32)
                for k in range(3):
                    u = 3 * par + k
                    b = u % 2
                    if not (isinstance(it, int) and it == 0 and u < 2):
                        pe.wait_ge(t_free[b], it * 3 + u // 2)
                    if k < 2:
                        for t in range(4):
                            mm = pe.transpose(ps[:, T_BANK[b], t * SLOT:(t + 1) * SLOT],
                                              xg[:, par, t, k * P:(k + 1) * P], idf[0:SLOT, 0:SLOT])
                    else:
                        for kk in range(KD):
                            mm = pe.transpose(ps[:, T_BANK[b], kk * LAST:(kk + 1) * LAST],
                                              xg[0:LAST, par, 4, kk * P:(kk + 1) * P], idf[0:LAST, 0:LAST])
                    mm.then_inc(t_full[b], 1)

            def hidden(it, par):
                e = it * 2 + par
                pe.wait_ge(s_xgl, e + 1)
                pe.wait_ge(s_wl, e * 16 + 16)
                for m in range(HM):
                    b0, b1 = (2 * m) % 4, (2 * m) % 4 + 1
                    if not (isinstance(e, int) and e == 0 and m < 2):
                        for b in (b0, b1):
                            pe.wait_ge(h_free[b], e * 4 + m // 2)
                    w = slice(m * P, (m + 1) * P)
                    n = 0
                    for k in range(KD):
                        wh, wl = hi(w1[:, par, k, w]), w1l[:, par, k, w]
                        xh, xl = hi(xgt[:, k, :]), xgl[:, k, :]
                        for l, r in ((wh, xh), (wh, xl), (wl, xh)):
                            ma = pe.matmul(ps[:, H_BANK[b0], 0:CA], l, r[:, 0:CA], start=(n == 0), stop=(n == 5))
                            mb = pe.matmul(ps[:, H_BANK[b1], 0:CB], l, r[:, CA:CAP], start=(n == 0), stop=(n == 5))
                            n += 1
                    ma.then_inc(h_full[b0], 1)
                    mb.then_inc(h_full[b1], 1)

            def second(it, par):
                e = it * 2 + par
                pe.wait_ge(s_hl, e * HM + HM)
                for t in range(ST5):
                    n = SLOT if t < 4 else LAST
                    u = ST5 * par + t
                    b = u % 2
                    if not (isinstance(it, int) and it == 0 and u < 2):
                        pe.wait_ge(y_free[b], it * 5 + u // 2)
                    s = slice(t * SLOT, t * SLOT + n)
                    o = ps[0:n, Y_BANK[b], 0:D]
                    for m in range(HM):
                        hh, hlo = hi(hrow(m)[:, s]), hl[:, m, s]
                        wh, wl = hi(w2[:, par, m, :]), w2l[:, par, m, :]
                        pe.matmul(o, hh, wh, start=(m == 0), stop=False)
                        pe.matmul(o, hh, wl, start=False, stop=False)
                        mm = pe.matmul(o, hlo, wh, start=False, stop=(m == HM - 1))
                    mm.then_inc(y_full[b], 1)

            turn_rows(0, 0)

            def expert(it, par, last=False):
                hidden(it, par)
                if not last:
                    turn_rows(it + par, 1 - par)
                second(it, par)

            expert(0, 0)
            expert(0, 1)
            with pe.Fori(1, E // 2 - 1) as it:
                expert(it, 0)
                expert(it, 1)
            expert(E // 2 - 1, 0)
            expert(E // 2 - 1, 1, last=True)


_OUT = (TOK + CAP, D)


def kernel(x, ctx_1024, mask_1x1xSxS2_ik1, g_xattn, g_ffn, L0_xattn_Wq, L0_xattn_bq, L0_xattn_Wk, L0_xattn_bk,
           L0_xattn_Wv, L0_xattn_bv, L0_xattn_Wo, L0_xattn_bo, L0_ffn_Wg, L0_ffn_W1, L0_ffn_b1, L0_ffn_W2, L0_ffn_b2):
    import concourse.bacc as bacc
    from concourse.bass_utils import run_bass_kernel_spmd

    f = np.float32
    ctxT = np.transpose(np.asarray(ctx_1024), (2, 0, 1))
    mask = np.asarray(mask_1x1xSxS2_ik1).reshape(S, KEYS)
    maskT = mask.T
    small = np.zeros((P, 128), f)
    small[:, 0:2] = np.asarray(L0_xattn_bq).reshape(KD, P).T
    small[:, 2:4] = np.asarray(L0_xattn_bk).reshape(KD, P).T
    small[:, 4] = np.asarray(g_xattn)[0]
    small[:, 5] = np.asarray(g_ffn)[0]
    small[:, 8:16] = np.arange(E, 0, -1)
    r = np.arange(P)[:, None] + ROWS * np.arange(3)[None, :]
    small[:, 16:19] = r < KEYS
    small[:, 19:22] = (r >= KEYS) & (r < 2 * KEYS)
    small[:, 24:28] = -0.5
    sel = np.zeros((2, HEADS, PAIRS, PK), np.uint16)
    for h in range(HEADS):
        sel[:, h, h // 2, (h % 2) * KEYS:(h % 2 + 1) * KEYS] = 0x3F80
    tok = np.arange(NT)[None, :] * P + np.arange(P)[:, None]
    empty = np.zeros((CAP, XW), f)
    empty[:, D] = (TOK + np.arange(CAP)).astype(np.int32).view(f)
    arrays = {
        "x": np.asarray(x).reshape(TOK, D),
        "ctxT": np.concatenate([ctxT, ctxT, ctxT[:, :, 0:PK - 2 * KEYS]], axis=2),
        "mask": mask,
        "maskT": np.concatenate([maskT, maskT, maskT[0:PK - 2 * KEYS]], axis=0),
        "WqT": np.asarray(L0_xattn_Wq).T, "WkT": np.asarray(L0_xattn_Wk).T,
        "WvT": np.asarray(L0_xattn_Wv).T, "WoT": np.asarray(L0_xattn_Wo).T,
        "bv": np.asarray(L0_xattn_bv), "bo": np.asarray(L0_xattn_bo),
        "Wg": np.asarray(L0_ffn_Wg),
        "W1": np.asarray(L0_ffn_W1).reshape(E * D, HID),
        "W2": np.asarray(L0_ffn_W2).reshape(E * HID, D),
        "b1T": np.asarray(L0_ffn_b1).reshape(E * HM, P).T,
        "b2": np.asarray(L0_ffn_b2).reshape(E * D),
        "small": small,
        "ident": np.eye(P, dtype=f),
        "before": np.triu(np.ones((P, P), f), 1),
        "shift_sel": sel.reshape(2 * HEADS, PAIRS, PK),
        "tokid": tok.astype(np.int32),
        "dump": np.stack([NSLOT + 2 * tok, NSLOT + 2 * tok + 1], axis=1).astype(f),
        "empty": empty,
    }
    arrays = {k: np.ascontiguousarray(v) for k, v in arrays.items()}
    nc = bacc.Bacc("TRN2", target_bir_lowering=False, num_devices=1)
    aps = {k: nc.dram_tensor("in_" + k, v.shape, mybir.dt.from_np(v.dtype), kind="ExternalInput").ap()
           for k, v in arrays.items()}
    aps["out"] = nc.dram_tensor("out_y", _OUT, F32, kind="ExternalOutput").ap()
    build(nc, aps)
    r = run_bass_kernel_spmd(nc, [{"in_" + k: v for k, v in arrays.items()}], core_ids=[0])
    return r.results[0]["out_y"][0:TOK].reshape(B, S, D)
```
